# Optimizing a Trainium2 kernel written in Bass

```python
import numpy as np
import jax
import jax.numpy as jnp

def _softmax(x, axis=-1):
    return jax.nn.softmax(x, axis=axis)

def _gelu(x):
    return jax.nn.gelu(x, approximate=True)

def _silu(x):
    return jax.nn.silu(x)

def _sigmoid(x):
    return jax.nn.sigmoid(x)

def _layernorm(x, axis=-1, eps=1e-05):
    m = jnp.mean(x, axis=axis, keepdims=True)
    v = jnp.var(x, axis=axis, keepdims=True)
    return (x - m) / jnp.sqrt(v + eps)

def _scatter_add(tgt, idx, src, axis=0):
    return tgt.at[idx].add(src)

def _segment_sum(src, seg, n):
    return jax.ops.segment_sum(src, seg, n)
kernel_name = 'mk_xattn_seq_d2_seqx_r8_5adaed'

def setup_inputs(seed: int=0):
    np.random.seed(seed)
    _w = jnp.asarray

    def _rec_inputs():
        import jax
        import jax.numpy as jnp
        _rk = jax.random.key(seed)
        x = -1.394e-06 + 0.9999 * jax.random.normal(jax.random.fold_in(_rk, 1), (4, 256, 128), jnp.float32)
        _lenS = 256 - jax.random.randint(jax.random.fold_in(_rk, 7), (4,), 0, max(1, 256 // 4) + 1, jnp.int32)
        _lenS2 = 512 - jax.random.randint(jax.random.fold_in(_rk, 8), (4,), 0, max(1, 512 // 4) + 1, jnp.int32)
        _ctx_1024P = jax.random.normal(jax.random.fold_in(_rk, 11), (4, 16, 128), jnp.float32)
        _ctx_1024c = jax.random.dirichlet(jax.random.fold_in(_rk, 511), 0.3 * jnp.ones((16,), jnp.float32), (4, 512))
        _ctx_1024t = jnp.einsum('bsk,bkd->bsd', _ctx_1024c, _ctx_1024P)
        _ctx_1024t = _ctx_1024t * jax.lax.rsqrt(jnp.mean(jnp.square(_ctx_1024t)) + 1e-12) * 0.953939
        ctx_1024 = 0.000241658 + 0.999772 * (_ctx_1024t + 0.3 * jax.random.normal(jax.random.fold_in(_rk, 611), (4, 512, 128), jnp.float32))
        return (x, ctx_1024)
    x, ctx_1024 = _rec_inputs()

    def _L0_xattn_setup():
        import jax, jax.numpy as jnp
        import numpy as np
        D = 128
        H = 16
        DF = 4 * D
        LQ, LKV, B = (256, 512, 2)
        EPS = 1e-05

        def _ln(x, g, b):
            mu = jnp.mean(x, axis=-1, keepdims=True)
            var = jnp.mean(jnp.square(x - mu), axis=-1, keepdims=True)
            return (x - mu) * jax.lax.rsqrt(var + EPS) * g + b

        def _mha(q, k, v, wq, wk, wv, wo):
            q = q @ wq.T
            k = k @ wk.T
            v = v @ wv.T
            b, lq, _ = q.shape
            lv = v.shape[1]
            qh = q.reshape(b, lq, H, -1).transpose(0, 2, 1, 3)
            kh = k.reshape(b, lv, H, -1).transpose(0, 2, 1, 3)
            vh = v.reshape(b, lv, H, -1).transpose(0, 2, 1, 3)
            dh = qh.shape[-1]
            scores = jnp.einsum('bhqd,bhkd->bhqk', qh, kh) / jnp.sqrt(jnp.float32(dh))
            attn = jax.nn.softmax(scores, axis=-1)
            o = jnp.einsum('bhqk,bhkd->bhqd', attn, vh)
            o = o.transpose(0, 2, 1, 3).reshape(b, lq, -1)
            return o @ wo.T
        key = jax.random.key(seed)
        kid = [0]

        def nrm(shape, s=1.0):
            kid[0] += 1
            return jax.random.normal(jax.random.fold_in(key, kid[0]), shape, dtype=jnp.float32) * s
        inp = {'q': nrm((B, LQ, D)), 'k': nrm((B, LKV, D)), 'v': nrm((B, LKV, D)), 'sa_wq': nrm((D, D), 0.02), 'sa_wk': nrm((D, D), 0.02), 'sa_wv': nrm((D, D), 0.02), 'sa_wo': nrm((D, D), 0.02), 'ca_wq': nrm((D, D), 0.02), 'ca_wk': nrm((D, D), 0.02), 'ca_wv': nrm((D, D), 0.02), 'ca_wo': nrm((D, D), 0.02), 'g_sa': jnp.ones((D,), jnp.float32), 'b_sa': jnp.zeros((D,), jnp.float32), 'g_qca': jnp.ones((D,), jnp.float32), 'b_qca': jnp.zeros((D,), jnp.float32), 'g_kca': jnp.ones((D,), jnp.float32), 'b_kca': jnp.zeros((D,), jnp.float32), 'g_vca': jnp.ones((D,), jnp.float32), 'b_vca': jnp.zeros((D,), jnp.float32), 'g_out': jnp.ones((D,), jnp.float32), 'b_out': jnp.zeros((D,), jnp.float32), 'ffn_w1': nrm((DF, D), 0.02), 'ffn_b1': jnp.zeros((DF,), jnp.float32), 'ffn_w2': nrm((D, DF), 0.02), 'ffn_b2': jnp.zeros((D,), jnp.float32)}
        return inp
    _L0_xattn_all = _L0_xattn_setup()
    _L0_xattn_in = {k: v for k, v in _L0_xattn_all.items() if k in ('sa_wq', 'sa_wk', 'sa_wv', 'sa_wo', 'ca_wq', 'ca_wk', 'ca_wv', 'ca_wo', 'g_sa', 'b_sa', 'g_qca', 'b_qca', 'g_kca', 'b_kca', 'g_vca', 'b_vca', 'g_out', 'b_out', 'ffn_w1', 'ffn_b1', 'ffn_w2', 'ffn_b2')}
    del _L0_xattn_all

    def _L1_xattn_setup():
        import jax, jax.numpy as jnp
        import numpy as np
        MODEL_DIM = 128
        HEAD_SIZE = 64
        N_HEADS = MODEL_DIM // HEAD_SIZE
        HIDDEN = 4 * MODEL_DIM
        B, S = (4, 256)

        def _mha(x, ctx, wq, wk, wv, wo):
            b, s, d = x.shape
            t = ctx.shape[1]
            q = (x @ wq).reshape(b, s, N_HEADS, HEAD_SIZE)
            k = (ctx @ wk).reshape(b, t, N_HEADS, HEAD_SIZE)
            v = (ctx @ wv).reshape(b, t, N_HEADS, HEAD_SIZE)
            scores = jnp.einsum('bqhd,bkhd->bhqk', q, k) / jnp.sqrt(jnp.float32(HEAD_SIZE)).astype(x.dtype)
            attn = jax.nn.softmax(scores, axis=-1)
            out = jnp.einsum('bhqk,bkhd->bqhd', attn, v).reshape(b, s, d)
            return out @ wo

        def _swiglu(x, wg, wu, wd):
            return jax.nn.silu(x @ wg) * (x @ wu) @ wd
        key = jax.random.key(seed)
        ks = jax.random.split(key, 20)
        sc = 0.02
        d, h = (MODEL_DIM, HIDDEN)
        return {'x': jax.random.normal(ks[0], (B, S, d), dtype=jnp.float32), 'y': jax.random.normal(ks[1], (B, S, d), dtype=jnp.float32), 'sa_wq': jax.random.normal(ks[2], (d, d), dtype=jnp.float32) * sc, 'sa_wk': jax.random.normal(ks[3], (d, d), dtype=jnp.float32) * sc, 'sa_wv': jax.random.normal(ks[4], (d, d), dtype=jnp.float32) * sc, 'sa_wo': jax.random.normal(ks[5], (d, d), dtype=jnp.float32) * sc, 'samlp_wg': jax.random.normal(ks[6], (d, h), dtype=jnp.float32) * sc, 'samlp_wu': jax.random.normal(ks[7], (d, h), dtype=jnp.float32) * sc, 'samlp_wd': jax.random.normal(ks[8], (h, d), dtype=jnp.float32) * sc, 'ca_wq': jax.random.normal(ks[9], (d, d), dtype=jnp.float32) * sc, 'ca_wk': jax.random.normal(ks[10], (d, d), dtype=jnp.float32) * sc, 'ca_wv': jax.random.normal(ks[11], (d, d), dtype=jnp.float32) * sc, 'ca_wo': jax.random.normal(ks[12], (d, d), dtype=jnp.float32) * sc, 'camlp_wg': jax.random.normal(ks[13], (d, h), dtype=jnp.float32) * sc, 'camlp_wu': jax.random.normal(ks[14], (d, h), dtype=jnp.float32) * sc, 'camlp_wd': jax.random.normal(ks[15], (h, d), dtype=jnp.float32) * sc}
    _L1_xattn_all = _L1_xattn_setup()
    _L1_xattn_in = {k: v for k, v in _L1_xattn_all.items() if k in ('sa_wq', 'sa_wk', 'sa_wv', 'sa_wo', 'samlp_wg', 'samlp_wu', 'samlp_wd', 'ca_wq', 'ca_wk', 'ca_wv', 'ca_wo', 'camlp_wg', 'camlp_wu', 'camlp_wd')}
    del _L1_xattn_all
    return {'x': x, 'ctx_1024': ctx_1024, 'L0_xattn_sa_wq': _L0_xattn_in['sa_wq'], 'L0_xattn_sa_wk': _L0_xattn_in['sa_wk'], 'L0_xattn_sa_wv': _L0_xattn_in['sa_wv'], 'L0_xattn_sa_wo': _L0_xattn_in['sa_wo'], 'L0_xattn_ca_wq': _L0_xattn_in['ca_wq'], 'L0_xattn_ca_wk': _L0_xattn_in['ca_wk'], 'L0_xattn_ca_wv': _L0_xattn_in['ca_wv'], 'L0_xattn_ca_wo': _L0_xattn_in['ca_wo'], 'L0_xattn_g_sa': _L0_xattn_in['g_sa'], 'L0_xattn_b_sa': _L0_xattn_in['b_sa'], 'L0_xattn_g_qca': _L0_xattn_in['g_qca'], 'L0_xattn_b_qca': _L0_xattn_in['b_qca'], 'L0_xattn_g_kca': _L0_xattn_in['g_kca'], 'L0_xattn_b_kca': _L0_xattn_in['b_kca'], 'L0_xattn_g_vca': _L0_xattn_in['g_vca'], 'L0_xattn_b_vca': _L0_xattn_in['b_vca'], 'L0_xattn_g_out': _L0_xattn_in['g_out'], 'L0_xattn_b_out': _L0_xattn_in['b_out'], 'L0_xattn_ffn_w1': _L0_xattn_in['ffn_w1'], 'L0_xattn_ffn_b1': _L0_xattn_in['ffn_b1'], 'L0_xattn_ffn_w2': _L0_xattn_in['ffn_w2'], 'L0_xattn_ffn_b2': _L0_xattn_in['ffn_b2'], 'L1_xattn_sa_wq': _L1_xattn_in['sa_wq'], 'L1_xattn_sa_wk': _L1_xattn_in['sa_wk'], 'L1_xattn_sa_wv': _L1_xattn_in['sa_wv'], 'L1_xattn_sa_wo': _L1_xattn_in['sa_wo'], 'L1_xattn_samlp_wg': _L1_xattn_in['samlp_wg'], 'L1_xattn_samlp_wu': _L1_xattn_in['samlp_wu'], 'L1_xattn_samlp_wd': _L1_xattn_in['samlp_wd'], 'L1_xattn_ca_wq': _L1_xattn_in['ca_wq'], 'L1_xattn_ca_wk': _L1_xattn_in['ca_wk'], 'L1_xattn_ca_wv': _L1_xattn_in['ca_wv'], 'L1_xattn_ca_wo': _L1_xattn_in['ca_wo'], 'L1_xattn_camlp_wg': _L1_xattn_in['camlp_wg'], 'L1_xattn_camlp_wu': _L1_xattn_in['camlp_wu'], 'L1_xattn_camlp_wd': _L1_xattn_in['camlp_wd']}

def reference(x, ctx_1024, L0_xattn_sa_wq, L0_xattn_sa_wk, L0_xattn_sa_wv, L0_xattn_sa_wo, L0_xattn_ca_wq, L0_xattn_ca_wk, L0_xattn_ca_wv, L0_xattn_ca_wo, L0_xattn_g_sa, L0_xattn_b_sa, L0_xattn_g_qca, L0_xattn_b_qca, L0_xattn_g_kca, L0_xattn_b_kca, L0_xattn_g_vca, L0_xattn_b_vca, L0_xattn_g_out, L0_xattn_b_out, L0_xattn_ffn_w1, L0_xattn_ffn_b1, L0_xattn_ffn_w2, L0_xattn_ffn_b2, L1_xattn_sa_wq, L1_xattn_sa_wk, L1_xattn_sa_wv, L1_xattn_sa_wo, L1_xattn_samlp_wg, L1_xattn_samlp_wu, L1_xattn_samlp_wd, L1_xattn_ca_wq, L1_xattn_ca_wk, L1_xattn_ca_wv, L1_xattn_ca_wo, L1_xattn_camlp_wg, L1_xattn_camlp_wu, L1_xattn_camlp_wd):
    import jax
    import jax.numpy as jnp

    def _L0_xattn_ref(q, k, v, sa_wq, sa_wk, sa_wv, sa_wo, ca_wq, ca_wk, ca_wv, ca_wo, g_sa, b_sa, g_qca, b_qca, g_kca, b_kca, g_vca, b_vca, g_out, b_out, ffn_w1, ffn_b1, ffn_w2, ffn_b2):
        import jax, jax.numpy as jnp
        import numpy as np
        D = 128
        H = 16
        DF = 4 * D
        LQ, LKV, B = (256, 512, 2)
        EPS = 1e-05

        def _ln(x, g, b):
            mu = jnp.mean(x, axis=-1, keepdims=True)
            var = jnp.mean(jnp.square(x - mu), axis=-1, keepdims=True)
            return (x - mu) * jax.lax.rsqrt(var + EPS) * g + b

        def _mha(q, k, v, wq, wk, wv, wo):
            q = q @ wq.T
            k = k @ wk.T
            v = v @ wv.T
            b, lq, _ = q.shape
            lv = v.shape[1]
            qh = q.reshape(b, lq, H, -1).transpose(0, 2, 1, 3)
            kh = k.reshape(b, lv, H, -1).transpose(0, 2, 1, 3)
            vh = v.reshape(b, lv, H, -1).transpose(0, 2, 1, 3)
            dh = qh.shape[-1]
            scores = jnp.einsum('bhqd,bhkd->bhqk', qh, kh) / jnp.sqrt(jnp.float32(dh))
            attn = jax.nn.softmax(scores, axis=-1)
            o = jnp.einsum('bhqk,bhkd->bhqd', attn, vh)
            o = o.transpose(0, 2, 1, 3).reshape(b, lq, -1)
            return o @ wo.T
        q = _ln(q, g_sa, b_sa)
        q = q + _mha(q, q, q, sa_wq, sa_wk, sa_wv, sa_wo)
        q = _ln(q, g_qca, b_qca)
        k = _ln(k, g_kca, b_kca)
        v = _ln(v, g_vca, b_vca)
        q = q[..., :D] + _mha(q, k, v, ca_wq, ca_wk, ca_wv, ca_wo)
        h = _ln(q, g_out, b_out)
        h = jax.nn.relu(h @ ffn_w1.T + ffn_b1) @ ffn_w2.T + ffn_b2
        return q + h

    def _L1_xattn_ref(x, y, sa_wq, sa_wk, sa_wv, sa_wo, samlp_wg, samlp_wu, samlp_wd, ca_wq, ca_wk, ca_wv, ca_wo, camlp_wg, camlp_wu, camlp_wd):
        import jax, jax.numpy as jnp
        import numpy as np
        MODEL_DIM = 128
        HEAD_SIZE = 64
        N_HEADS = MODEL_DIM // HEAD_SIZE
        HIDDEN = 4 * MODEL_DIM
        B, S = (4, 256)

        def _mha(x, ctx, wq, wk, wv, wo):
            b, s, d = x.shape
            t = ctx.shape[1]
            q = (x @ wq).reshape(b, s, N_HEADS, HEAD_SIZE)
            k = (ctx @ wk).reshape(b, t, N_HEADS, HEAD_SIZE)
            v = (ctx @ wv).reshape(b, t, N_HEADS, HEAD_SIZE)
            scores = jnp.einsum('bqhd,bkhd->bhqk', q, k) / jnp.sqrt(jnp.float32(HEAD_SIZE)).astype(x.dtype)
            attn = jax.nn.softmax(scores, axis=-1)
            out = jnp.einsum('bhqk,bkhd->bqhd', attn, v).reshape(b, s, d)
            return out @ wo

        def _swiglu(x, wg, wu, wd):
            return jax.nn.silu(x @ wg) * (x @ wu) @ wd
        x = x + _mha(x, x, sa_wq, sa_wk, sa_wv, sa_wo)
        x = x + _swiglu(x, samlp_wg, samlp_wu, samlp_wd)
        x = x + _mha(x, y, ca_wq, ca_wk, ca_wv, ca_wo)
        x = x + _swiglu(x, camlp_wg, camlp_wu, camlp_wd)
        return x
    x = _L0_xattn_ref(x, ctx_1024, ctx_1024, L0_xattn_sa_wq, L0_xattn_sa_wk, L0_xattn_sa_wv, L0_xattn_sa_wo, L0_xattn_ca_wq, L0_xattn_ca_wk, L0_xattn_ca_wv, L0_xattn_ca_wo, L0_xattn_g_sa, L0_xattn_b_sa, L0_xattn_g_qca, L0_xattn_b_qca, L0_xattn_g_kca, L0_xattn_b_kca, L0_xattn_g_vca, L0_xattn_b_vca, L0_xattn_g_out, L0_xattn_b_out, L0_xattn_ffn_w1, L0_xattn_ffn_b1, L0_xattn_ffn_w2, L0_xattn_ffn_b2)
    x = _L1_xattn_ref(x, ctx_1024, L1_xattn_sa_wq, L1_xattn_sa_wk, L1_xattn_sa_wv, L1_xattn_sa_wo, L1_xattn_samlp_wg, L1_xattn_samlp_wu, L1_xattn_samlp_wd, L1_xattn_ca_wq, L1_xattn_ca_wk, L1_xattn_ca_wv, L1_xattn_ca_wo, L1_xattn_camlp_wg, L1_xattn_camlp_wu, L1_xattn_camlp_wd)
    return x

_drawn_inputs = setup_inputs


def setup_inputs(seed=0):
    import zlib

    import numpy as np

    out = dict(_drawn_inputs(seed))
    spreads = {'L0_xattn_g_sa': (1.0, 0.2),
     'L0_xattn_b_sa': (0.0, 0.1),
     'L0_xattn_g_qca': (1.0, 0.2),
     'L0_xattn_b_qca': (0.0, 0.1),
     'L0_xattn_g_kca': (1.0, 0.6),
     'L0_xattn_b_kca': (0.0, 2.0),
     'L0_xattn_g_vca': (1.0, 0.6),
     'L0_xattn_b_vca': (0.0, 0.8),
     'L0_xattn_g_out': (1.0, 0.6),
     'L0_xattn_b_out': (0.0, 0.8),
     'L0_xattn_ffn_b1': (0.0, 0.291),
     'L0_xattn_ffn_b2': (0.0, 0.1)}
    factors = {'L0_xattn_sa_wq': 8.0,
     'L0_xattn_sa_wk': 8.0,
     'L0_xattn_sa_wv': 8.0,
     'L0_xattn_sa_wo': 8.0,
     'L0_xattn_ca_wq': 8.0,
     'L0_xattn_ca_wk': 8.0,
     'L1_xattn_sa_wq': 8.0,
     'L1_xattn_sa_wk': 8.0,
     'L1_xattn_sa_wv': 6.063,
     'L1_xattn_sa_wo': 6.711,
     'L1_xattn_samlp_wg': 4.601,
     'L1_xattn_samlp_wu': 4.603,
     'L1_xattn_samlp_wd': 4.562,
     'L1_xattn_ca_wq': 32.32,
     'L1_xattn_ca_wk': 32.34,
     'L1_xattn_camlp_wg': 4.523,
     'L1_xattn_camlp_wu': 4.459,
     'L1_xattn_camlp_wd': 4.46,
     'L1_xattn_ca_wv': 3.733,
     'L1_xattn_ca_wo': 3.777}
    for name, (base, spread) in spreads.items():
        noise = np.random.default_rng([zlib.crc32(name.encode()), seed]).standard_normal(out[name].shape)
        drawn = base * np.exp(spread * noise) if base else spread * noise
        out[name] = jnp.asarray(drawn.astype(out[name].dtype))
    for name, factor in factors.items():
        out[name] = (out[name] * factor).astype(out[name].dtype)
    return out
```

```python
import concourse.bass as bass
from concourse import mybir
from contextlib import ExitStack

B, TQ, TC, D = 4, 256, 512, 128
H0, DH0 = 16, 8
H1, DH1 = 2, 64
DF = 4 * D
EPS = 1e-5
P = 128
QT = TQ // P
GROUP = 4
GROUPS = H0 // GROUP
PAIRS = H0 // 2
PRODUCTS = 6
STACK = PRODUCTS * 2 * DH0
ROWS = STACK + 6
Q_PART = (0, 0, 0, 1, 1, 2)
K_PART = (0, 1, 2, 0, 1, 0)
SLAB_ORDER = (0, 1, 3, 2, 4, 5)
V_WIDTH = 32
T_KEYS = {"self": TQ, "cross": TC}
TILES = {u: GROUP * QT * T_KEYS[u] // 512 for u in T_KEYS}

WEIGHTS = (
    ("self_wq", 1), ("self_wk", 1), ("self_wv", 1), ("cross_wk", 1), ("cross_wv", 1),
    ("self_wo", 1), ("cross_wq", 1), ("cross_wo", 1), ("w1", 4), ("w2", 4),
    ("b_self_wq", 1), ("b_self_wk", 1), ("b_self_wv", 1), ("b_self_wo", 1),
    ("b_self_wg", 4), ("b_self_wu", 4), ("b_self_wd", 4),
    ("b_cross_wq", 1), ("b_cross_wk", 1), ("b_cross_wv", 1), ("b_cross_wo", 1),
    ("b_cross_wg", 4), ("b_cross_wu", 4), ("b_cross_wd", 4),
)
W_AT, _n = {}, 0
for _name, _k in WEIGHTS:
    W_AT[_name] = _n
    _n += _k
W_TILES = _n
W_FIRST = W_AT["self_wo"]
W_LAYER1 = W_AT["b_self_wq"]
VECTORS = ("g_in", "b_in", "g_k", "b_k", "g_v", "b_v", "g_mid", "b_mid", "g_out", "b_out", "b2", "b1")
V_AT = {n: i for i, n in enumerate(VECTORS)}
C_CENTRE, C_MEAN, C_IDENT, C_ONES, C_VEC = 0, P, 2 * P, 3 * P, 3 * P + 2
C_WIDTH = C_VEC + len(VECTORS) - 1 + DF // P



def attention_steps(u):
    return [("att", u, s, p) for s in range(-2, GROUPS + 1) for p in range(TILES[u])]


LAYER0 = (
    [("load",)]
    + [(k, n) for k in ("ln_centre", "ln_var", "ln_apply") for n in ("in", "ctx")]
    + [("q_proj", "self"), ("k_proj", "self"), ("v_proj", "self"), ("k_proj", "cross"), ("v_proj", "cross")]
    + attention_steps("self")
    + [("att_turn", "self"), ("att_norm", "self"), ("att_back", "self"), ("att_wo", "self")]
    + [("ln_centre", "mid"), ("ln_var", "mid"), ("ln_apply", "mid"), ("q_proj", "cross")]
    + attention_steps("cross")
    + [("att_turn", "cross"), ("att_norm", "cross"), ("att_back", "cross"), ("att_wo", "cross")]
    + [("ln_centre", "out"), ("ln_var", "out"), ("ln_apply", "out")]
    + [("ffn_up", 0), ("ffn_up", 1), ("ffn_down",)]
)


def layer1_half(u):
    n = QT * H1 * T_KEYS[u] // 512
    return (
        [("b_k", u), ("b_v", u), ("b_q", u)]
        + [("b_score", u, t) for t in range(n)]
        + [("b_norm", u, t) for t in range(n)]
        + [("b_turn", u, t) for t in range(n)]
        + [("b_pv", u), ("b_wo", u)]
        + [("b_mlp", u, 0), ("b_mlp", u, 1), ("b_down", u)]
    )


LAYER1 = [("b_load",)] + layer1_half("self") + layer1_half("cross") + [("b_store",)]


def weight(step):
    kind = step[0]
    if kind == "att":
        return 7
    if kind in ("load", "b_load", "b_store", "att_norm"):
        return 0
    if kind in ("b_mlp",):
        return 17
    if kind in ("b_down", "ffn_up", "ffn_down"):
        return 17
    if kind in ("b_score",):
        return 9
    return 8


def merged():
    total0, total1 = sum(map(weight, LAYER0)), sum(map(weight, LAYER1))
    out, n, done0, done1 = [], 0, 0, 0
    for step in LAYER0:
        while n < len(LAYER1) and done1 * total0 <= done0 * total1:
            out.append((1, LAYER1[n]))
            done1 += weight(LAYER1[n])
            n += 1
        out.append((0, step))
        done0 += weight(step)
    return out + [(1, s) for s in LAYER1[n:]]


MERGED = merged()


class Signal:

    def __init__(self, sem, per, first=0, own=None, credit=0):
        self.sem, self.per, self.first, self.own = sem, per, first, per if own is None else own
        self.credit = credit

    def at(self, i, k):
        return i * self.per + (self.credit + self.first + k)

    def before(self, i):
        return i * self.per + (self.credit + self.first + self.own - self.per)


def two_layers(nc, x_t, ctx_t, w_all, c_all, out_t):
    fp32, bf16, u32 = mybir.dt.float32, mybir.dt.bfloat16, mybir.dt.uint32
    ALU = mybir.AluOpType
    ACT = mybir.ActivationFunctionType
    AX = mybir.AxisListType.X
    ctx = ExitStack()
    with ctx:
        def sb(name, shape, dt=fp32):
            return ctx.enter_context(nc.sbuf_tensor(name, shape, dt))

        def signal(name, per):
            return Signal(ctx.enter_context(nc.semaphore(name)), per)

        def shared(name, credit=0, **own):
            sem, first, stages = ctx.enter_context(nc.semaphore(name)), 0, {}
            for stage, n in own.items():
                stages[stage] = Signal(sem, sum(own.values()), first, n, credit)
                first += n
            return stages

        W = sb("weights", [P, W_TILES, P])
        C = sb("constants", [P, C_WIDTH])
        ident16 = sb("ident16", [P, P], bf16)
        eps = sb("eps", [P, 1])
        zeros = sb("zeros", [P, QT, GROUP])
        x_in = sb("x_in", [P, TQ])
        c_in = sb("c_in", [P, TC])
        LN_N = {"in": TQ, "ctx": TC, "mid": TQ, "out": TQ}
        square = {n: sb(f"square_{n}", [P, LN_N[n]]) for n in LN_N}
        logvar = {n: sb(f"logvar_{n}", [P, LN_N[n]]) for n in LN_N}
        rstd = {n: sb(f"rstd_{n}", [P, LN_N[n]]) for n in LN_N}
        unit = {n: sb(f"unit_{n}", [P, LN_N[n]]) for n in LN_N}
        normed = {n: sb(f"normed_{n}", [P, TQ]) for n in ("in", "mid", "out")}
        k_in = sb("k_in", [P, TC])
        v_in = sb("v_in", [P, TC])
        q_part = {u: [sb(f"q_part_{u}{j}", [P, TQ], bf16) for j in range(3)] for u in T_KEYS}
        k_part = {u: [sb(f"k_part_{u}{j}", [P, T_KEYS[u]], bf16) for j in range(3)] for u in T_KEYS}
        q_rest = {u: sb(f"q_rest_{u}", [P, TQ]) for u in T_KEYS}
        k_rest = {u: sb(f"k_rest_{u}", [P, T_KEYS[u]]) for u in T_KEYS}
        q_stack = {u: sb(f"q_stack_{u}", [P, PAIRS, TQ], bf16) for u in T_KEYS}
        k_stack = {u: sb(f"k_stack_{u}", [P, PAIRS, 2, T_KEYS[u]], bf16) for u in T_KEYS}
        v_ones = {u: sb(f"v_ones_{u}", [P, T_KEYS[u] // P, H0, V_WIDTH]) for u in T_KEYS}
        neg_max = sb("neg_max", [P, 2, QT, GROUP])
        neg_rest = sb("neg_rest", [P, 2, QT, GROUP])
        neg_part = sb("neg_part", [P, 2, QT, GROUP, 3], bf16)
        probs_t = sb("probs_t", [P, 2, GROUP, TC // P, TQ])
        heads_t = sb("heads_t", [P, GROUPS, TQ])
        recip = sb("recip", [P, QT, H0])
        heads = sb("heads", [P, QT, H0, DH0])
        heads_f = sb("heads_f", [P, TQ])
        attended = {u: sb(f"attended_{u}", [P, TQ]) for u in T_KEYS}
        hidden = sb("hidden", [P, DF // P, TQ])
        x_mid = sb("x_mid", [P, TQ])
        ctx1 = sb("ctx1", [P, TC])
        bq = sb("bq", [P, TQ])
        bk = sb("bk", [P, TC])
        bv = sb("bv", [P, TC // P, P])
        b_neg = sb("b_neg", [P, H1, QT])
        b_sum = sb("b_sum", [P, H1, QT])
        b_rec = sb("b_rec", [P, H1, QT])
        b_probs = sb("b_probs", [P, H1, QT, TC])
        b_probs_t = sb("b_probs_t", [P, H1, TC // P, TQ])
        b_heads = sb("b_heads", [P, TQ])
        b_attended = {u: sb(f"b_attended_{u}", [P, TQ]) for u in T_KEYS}
        b_exp = sb("b_exp", [P, 2, 2 * TQ])
        b_gate = sb("b_gate", [P, 2, 2 * TQ])
        b_hidden = sb("b_hidden", [P, DF // P, TQ])
        b_out = {u: sb(f"b_out_{u}", [P, TQ]) for u in T_KEYS}
        ps = ctx.enter_context(nc.psum_tensor("ps", [P, 8, 512], fp32))
        neg_rows = ps[:, 5, :].bitcast(bf16)

        centre, mean, ident = C[:, C_CENTRE:C_CENTRE + P], C[:, C_MEAN:C_MEAN + P], C[:, C_IDENT:C_IDENT + P]

        def w(name, tile=0):
            return W[:, W_AT[name] + tile, :]

        def vec(name, col=0):
            at = C_VEC + V_AT[name] + col
            return C[:, at:at + 1]

        def by_norm(name, ctx_own=1):
            return {"ctx": signal(f"{name}_ctx", ctx_own), **shared(name, **{"in": 1, "mid": 1, "out": 1})}

        US = ("self", "cross")
        const_loaded = signal("const_loaded", 0)
        w_first_loaded = signal("w_first_loaded", 0)
        w_rest_loaded = signal("w_rest_loaded", 0)
        w_layer1_loaded = signal("w_layer1_loaded", 0)
        stacks_clear = signal("stacks_clear", 0)
        stacks_set = signal("stacks_set", 0)
        ones_set = signal("ones_set", 0)
        eps_set = signal("eps_set", 0)
        zeros_set = signal("zeros_set", 0)
        v_clear = signal("v_clear", 0)
        x_loaded = signal("x_loaded", 16)
        c_loaded = signal("c_loaded", 16)
        centred = by_norm("centred")
        squared = by_norm("squared")
        variance = by_norm("variance")
        logged = by_norm("logged")
        rooted = by_norm("rooted")
        scaled = by_norm("scaled")
        affine = by_norm("affine", 2)
        q_made = shared("q_made", self=1, cross=1)
        k_made = shared("k_made", self=1, cross=1)
        v_made = shared("v_made", self=1, cross=1)
        q_first = shared("q_first", self=1, cross=1)
        k_first = shared("k_first", self=1, cross=1)
        q_less = shared("q_less", self=1, cross=1)
        k_less = shared("k_less", self=1, cross=1)
        q_split = shared("q_split", self=2, cross=2)
        k_split = shared("k_split", self=2, cross=2)
        v_kept = shared("v_kept", self=1, cross=1)
        q_stacked = shared("q_stacked", self=16 * PRODUCTS, cross=16 * PRODUCTS)
        k_stacked = {u: signal(f"k_stacked_{u}", 32 * PRODUCTS) for u in US}
        scores = shared("scores", self=TILES["self"] * GROUPS, cross=TILES["cross"] * GROUPS)
        maxed = shared("maxed", self=TILES["self"] * GROUPS, cross=TILES["cross"] * GROUPS)
        neg_1 = shared("neg_1", self=GROUPS, cross=GROUPS)
        neg_2 = shared("neg_2", self=GROUPS, cross=GROUPS)
        neg_3 = shared("neg_3", self=GROUPS, cross=GROUPS)
        neg_split = shared("neg_split", self=GROUPS, cross=GROUPS)
        neg_turned = shared("neg_turned", self=GROUPS, cross=GROUPS)
        neg_placed = shared("neg_placed", self=GROUPS, cross=GROUPS)
        scores_t = shared("scores_t", self=TILES["self"] * GROUPS, cross=TILES["cross"] * GROUPS)
        exped = shared("exped", self=TILES["self"] * GROUPS, cross=TILES["cross"] * GROUPS)
        weighted = shared("weighted", self=GROUPS, cross=GROUPS)
        heads_kept = shared("heads_kept", self=GROUPS, cross=GROUPS)
        heads_turned = shared("heads_turned", self=QT, cross=QT)
        inverted = shared("inverted", self=QT, cross=QT)
        divided = shared("divided", self=QT, cross=QT)
        heads_back = shared("heads_back", self=1, cross=1)
        heads_done = shared("heads_done", self=1, cross=1)
        projected = shared("projected", self=1, cross=1)
        residual = shared("residual", self=1, cross=1)
        ffn_made = signal("ffn_made", 2)
        ffn_kept = signal("ffn_kept", DF // P)
        ffn_summed = signal("ffn_summed", 1)
        layer0_done = signal("layer0_done", 1)
        ctx1_loaded = signal("ctx1_loaded", 16)
        N1 = {u: QT * H1 * T_KEYS[u] // 512 for u in US}
        b_q_made = shared("b_q_made", self=1, cross=1)
        b_k_made = shared("b_k_made", self=1, cross=1)
        b_v_made = shared("b_v_made", self=1, cross=1)
        b_q_kept = shared("b_q_kept", self=1, cross=1)
        b_k_kept = shared("b_k_kept", self=1, cross=1)
        b_v_kept = shared("b_v_kept", credit=1, self=1, cross=1)
        b_scores = shared("b_scores", self=N1["self"], cross=N1["cross"])
        b_maxed = shared("b_maxed", self=N1["self"], cross=N1["cross"])
        b_exped = shared("b_exped", self=H1 * QT, cross=H1 * QT)
        b_inverted = shared("b_inverted", self=H1, cross=H1)
        b_normed = shared("b_normed", self=H1 * QT, cross=H1 * QT)
        b_turned = shared("b_turned", self=N1["self"], cross=N1["cross"])
        b_turned_kept = shared("b_turned_kept", self=N1["self"], cross=N1["cross"])
        b_weighted = shared("b_weighted", self=1, cross=1)
        b_heads_kept = shared("b_heads_kept", self=1, cross=1)
        b_projected = shared("b_projected", self=1, cross=1)
        b_residual = shared("b_residual", self=1, cross=1)
        b_gate_made = shared("b_gate_made", self=2, cross=2)
        b_up_made = shared("b_up_made", self=2, cross=2)
        b_gate_exp = shared("b_gate_exp", self=2, cross=2)
        b_gate_one = shared("b_gate_one", self=2, cross=2)
        b_gate_inv = shared("b_gate_inv", self=2, cross=2)
        b_gate_silu = shared("b_gate_silu", self=2, cross=2)
        b_hidden_kept = shared("b_hidden_kept", self=2, cross=2)
        b_down_made = shared("b_down_made", self=1, cross=1)
        b_done = shared("b_done", credit=1, self=1, cross=1)
        stored = shared("stored", credit=16, store=16)["store"]

        LN_SRC = {"in": (x_in, x_loaded, 16), "ctx": (c_in, c_loaded, 16),
                  "mid": (attended["self"], residual["self"], 1), "out": (attended["cross"], residual["cross"], 1)}

        def ln_banks(n):
            if n == "ctx":
                return ps[:, 0, :], ps[:, 1, :]
            return ps[:, 5, 0:TQ], ps[:, 5, TQ:2 * TQ]

        Q_SRC = {"self": (normed["in"], affine["in"]), "cross": (normed["mid"], affine["mid"])}
        K_SRC = {"self": (normed["in"], affine["in"]), "cross": (k_in, affine["ctx"])}
        V_SRC = {"self": (normed["in"], affine["in"]), "cross": (v_in, affine["ctx"])}

        def q_bank(u):
            return ps[:, 2, 0:TQ]

        def k_bank(u):
            return ps[:, 3, 0:TQ] if u == "self" else ps[:, 0, :]

        def v_bank(u):
            return ps[:, 4, 0:TQ] if u == "self" else ps[:, 1, :]

        def b_k_bank(u):
            return ps[:, 6, 0:T_KEYS[u]]

        def b_v_bank(u):
            return ps[:, 7, 0:T_KEYS[u]].rearrange("p (t f) -> p t f", f=P)

        def b_q_bank(u):
            return ps[:, 6, TQ:2 * TQ] if u == "self" else ps[:, 6, 0:TQ]

        def b_tile(u, t):
            return [(t, qt) for qt in range(QT)] if u == "self" else [(t // QT, t % QT)]

        def b_score_bank(u, t, qt):
            return ps[:, 6 + t % 2, qt * TQ:(qt + 1) * TQ] if u == "self" else ps[:, 6 + t % 2, :]

        def reuse(eng, sig, i):
            if not (isinstance(i, int) and i == 0):
                eng.wait_ge(sig.sem, sig.before(i))

        def run(eng, steps):
            for kind, *args in LAYER0:
                if kind in steps:
                    steps[kind](0, *args)
            with eng.Fori(1, B) as b:
                for layer, (kind, *args) in MERGED:
                    if kind in steps:
                        steps[kind](b - 1 if layer else b, *args)
            for kind, *args in LAYER1:
                if kind in steps:
                    steps[kind](B - 1, *args)

        block = ctx.enter_context(nc.Block())

        @block.sync
        def _(sp):
            sp.dma_start(C[:, :], c_all).then_inc(const_loaded.sem, 16)
            sp.sem_inc(stored.sem, stored.credit)

            def load(i):
                reuse(sp, centred["in"], i)
                sp.dma_start(x_in[:, :], x_t[:, bass.ds(i * TQ, TQ)]).then_inc(x_loaded.sem, 16)
                reuse(sp, centred["ctx"], i)
                sp.dma_start(c_in[:, :], ctx_t[:, bass.ds(i * TC, TC)]).then_inc(c_loaded.sem, 16)
                if isinstance(i, int):
                    w_view = w_all.rearrange("p (t n) -> p t n", n=P)
                    sp.dma_start(W[:, 0:W_FIRST, :], w_view[:, 0:W_FIRST, :]).then_inc(w_first_loaded.sem, 16)
                    sp.dma_start(W[:, W_FIRST:W_LAYER1, :], w_view[:, W_FIRST:W_LAYER1, :]).then_inc(w_rest_loaded.sem, 16)
                    sp.dma_start(W[:, W_LAYER1:, :], w_view[:, W_LAYER1:, :]).then_inc(w_layer1_loaded.sem, 16)
                    sp.wait_ge(stacks_clear.sem, 2)

            def part_ready(first, split, i, part):
                if part == 0:
                    sp.wait_ge(first.sem, first.at(i, 1))
                else:
                    sp.wait_ge(split.sem, split.at(i, part))

            def q_proj(i, u):
                for n in SLAB_ORDER:
                    part_ready(q_first[u], q_split[u], i, Q_PART[n])
                    sp.dma_start(q_stack[u][16 * n:16 * n + 16, :, :], q_part[u][Q_PART[n]][:, :])\
                        .then_inc(q_stacked[u].sem, 16)

            def k_proj(i, u):
                for n in (0, 3, 5, 1, 4, 2):
                    part_ready(k_first[u], k_split[u], i, K_PART[n])
                    for hh in range(2):
                        at = 16 * n + DH0 * hh
                        sp.dma_start(k_stack[u][at:at + DH0, :, hh, :],
                                     k_part[u][K_PART[n]][64 * hh:64 * hh + 64, :]).then_inc(k_stacked[u].sem, 16)

            def b_load(i):
                reuse(sp, b_v_kept["cross"], i)
                sp.dma_start(ctx1[:, :], ctx_t[:, bass.ds(i * TC, TC)]).then_inc(ctx1_loaded.sem, 16)

            def b_store(i):
                sp.wait_ge(b_done["cross"].sem, b_done["cross"].at(i, 1))
                sp.dma_start(out_t[:, bass.ds(i * TQ, TQ)], b_out["cross"][:, :]).then_inc(stored.sem, 16)

            run(sp, dict(load=load, q_proj=q_proj, k_proj=k_proj, b_load=b_load, b_store=b_store))
            sp.wait_ge(stored.sem, stored.at(B - 1, 16))

        @block.gpsimd
        def _(pool):
            nc.gpsimd.memset(k_stack["cross"][:].rearrange("p a b t -> p (a b t)").bitcast(u32), 0)\
                .then_inc(stacks_clear.sem, 1)
            nc.gpsimd.memset(zeros[:, :, :], 0.0).then_inc(zeros_set.sem, 1)
            pool.wait_ge(zeros_set.sem, 1)

            def att(i, u, s, p):
                g = s + 1
                if p or not 0 <= g < GROUPS:
                    return
                slot = g % 2
                neg, rest, part = neg_max[:, slot], neg_rest[:, slot], neg_part[:, slot]
                pool.wait_ge(maxed[u].sem, maxed[u].at(i, TILES[u] * (g + 1)))
                if g >= 2:
                    pool.wait_ge(neg_turned[u].sem, neg_turned[u].at(i, g - 1))
                nc.gpsimd.tensor_tensor(part[:, :, :, 0], neg, zeros[:, :, :], ALU.add).then_inc(neg_1[u].sem, 1)
                pool.wait_ge(neg_1[u].sem, neg_1[u].at(i, g + 1))
                nc.gpsimd.tensor_tensor(rest, neg, part[:, :, :, 0], ALU.subtract).then_inc(neg_2[u].sem, 1)
                pool.wait_ge(neg_2[u].sem, neg_2[u].at(i, g + 1))
                nc.gpsimd.tensor_tensor(part[:, :, :, 1], rest, zeros[:, :, :], ALU.add).then_inc(neg_3[u].sem, 1)
                pool.wait_ge(neg_3[u].sem, neg_3[u].at(i, g + 1))
                nc.gpsimd.tensor_tensor(part[:, :, :, 2], rest, part[:, :, :, 1], ALU.subtract)\
                    .then_inc(neg_split[u].sem, 1)

            run(pool, dict(att=att))

        @block.scalar
        def _(act):
            act.wait_ge(const_loaded.sem, 16)
            act.wait_ge(eps_set.sem, 1)

            def ln_centre(i, n):
                act.wait_ge(centred[n].sem, centred[n].at(i, 1))
                nc.scalar.activation(square[n][:, :], ln_banks(n)[0], ACT.Square).then_inc(squared[n].sem, 1)

            def ln_var(i, n):
                act.wait_ge(variance[n].sem, variance[n].at(i, 1))
                nc.scalar.activation(logvar[n][:, :], ln_banks(n)[1], ACT.Ln, bias=eps[:, :]).then_inc(logged[n].sem, 1)
                act.wait_ge(logged[n].sem, logged[n].at(i, 1))
                nc.scalar.activation(rstd[n][:, :], logvar[n][:, :], ACT.Exp, scale=-0.5).then_inc(rooted[n].sem, 1)

            def q_proj(i, u):
                act.wait_ge(q_made[u].sem, q_made[u].at(i, 1))
                nc.scalar.copy(q_part[u][0][:, :], q_bank(u)).then_inc(q_first[u].sem, 1)

            def k_proj(i, u):
                act.wait_ge(k_made[u].sem, k_made[u].at(i, 1))
                nc.scalar.copy(k_part[u][0][:, :], k_bank(u)).then_inc(k_first[u].sem, 1)

            def v_proj(i, u):
                act.wait_ge(v_made[u].sem, v_made[u].at(i, 1))
                if isinstance(i, int):
                    act.wait_ge(stacks_set.sem, 2)
                nc.scalar.copy(v_ones[u][:, :, :, 0:DH0],
                               v_bank(u).rearrange("p (t h d) -> p t h d", h=H0, d=DH0)).then_inc(v_kept[u].sem, 1)

            def keep_heads(i, u, g):
                act.wait_ge(weighted[u].sem, weighted[u].at(i, g + 1))
                nc.scalar.copy(heads_t[:, g, :], ps[:, 4, 0:TQ]).then_inc(heads_kept[u].sem, 1)

            def att(i, u, s, p):
                if p == 0 and 0 <= s - 2 < GROUPS:
                    keep_heads(i, u, s - 2)
                if not 0 <= s < GROUPS:
                    return
                n = s * TILES[u] + p
                if p == 0 and s >= 2:
                    act.wait_ge(weighted[u].sem, weighted[u].at(i, s - 1))
                act.wait_ge(scores_t[u].sem, scores_t[u].at(i, n + 1))
                per_head = T_KEYS[u] // 256
                kt = 2 * (p % per_head)
                nc.scalar.activation(probs_t[:, s % 2, p // per_head, kt:kt + 2, :],
                                     ps[:, 2 + n % 2, :].rearrange("p (t q) -> p t q", t=2),
                                     ACT.Exp, scale=DH0 ** -0.5).then_inc(exped[u].sem, 1)

            def att_turn(i, u):
                keep_heads(i, u, GROUPS - 1)

            def att_back(i, u):
                act.wait_ge(heads_back[u].sem, heads_back[u].at(i, 1))
                nc.scalar.copy(heads_f[:, :], ps[:, 5, 0:TQ]).then_inc(heads_done[u].sem, 1)

            def ffn_up(i, m):
                act.wait_ge(ffn_made.sem, ffn_made.at(i, m + 1))
                for t in range(2):
                    nc.scalar.activation(hidden[:, 2 * m + t, :], ps[:, m, t * TQ:(t + 1) * TQ], ACT.Relu,
                                         bias=vec("b1", 2 * m + t)).then_inc(ffn_kept.sem, 1)

            def b_q(i, u):
                act.wait_ge(b_q_made[u].sem, b_q_made[u].at(i, 1))
                nc.scalar.mul(bq[:, :], b_q_bank(u), DH1 ** -0.5).then_inc(b_q_kept[u].sem, 1)

            def b_k(i, u):
                act.wait_ge(b_k_made[u].sem, b_k_made[u].at(i, 1))
                nc.scalar.copy(bk[:, 0:T_KEYS[u]], b_k_bank(u)).then_inc(b_k_kept[u].sem, 1)

            def b_score(i, u, t):
                act.wait_ge(b_maxed[u].sem, b_maxed[u].at(i, t + 1))
                for h, qt in b_tile(u, t):
                    nc.scalar.activation(b_probs[:, h, qt, 0:T_KEYS[u]], b_score_bank(u, t, qt), ACT.Exp,
                                         bias=b_neg[:, h, qt:qt + 1], accum_out=b_sum[:, h, qt:qt + 1])\
                        .then_inc(b_exped[u].sem, 1)

            def b_turn(i, u, m):
                act.wait_ge(b_turned[u].sem, b_turned[u].at(i, m + 1))
                per_head = T_KEYS[u] // 256
                kt = 2 * (m % per_head)
                nc.scalar.copy(b_probs_t[:, m // per_head, kt:kt + 2, :],
                               ps[:, 6 + m % 2, :].rearrange("p (t q) -> p t q", t=2)).then_inc(b_turned_kept[u].sem, 1)

            def b_pv(i, u):
                act.wait_ge(b_weighted[u].sem, b_weighted[u].at(i, 1))
                nc.scalar.copy(b_heads[:, :], ps[:, 6, 0:TQ]).then_inc(b_heads_kept[u].sem, 1)

            def b_mlp(i, u, m):
                act.wait_ge(b_gate_made[u].sem, b_gate_made[u].at(i, m + 1))
                nc.scalar.activation(b_exp[:, m, :], ps[:, 6, :], ACT.Exp, scale=-1.0).then_inc(b_gate_exp[u].sem, 1)

            run(act, dict(ln_centre=ln_centre, ln_var=ln_var, q_proj=q_proj, k_proj=k_proj, v_proj=v_proj,
                          att=att, att_turn=att_turn, att_back=att_back, ffn_up=ffn_up, b_q=b_q, b_k=b_k,
                          b_score=b_score, b_turn=b_turn, b_pv=b_pv, b_mlp=b_mlp))

        @block.vector
        def _(dve):
            for credited in (b_v_kept["self"], b_done["self"]):
                dve.sem_inc(credited.sem, credited.credit)
            dve.wait_ge(const_loaded.sem, 16)
            nc.vector.tensor_copy(ident16[:, :], ident).then_inc(stacks_set.sem, 1)
            nc.vector.memset(eps[:, :], EPS).then_inc(eps_set.sem, 1)
            for u in US:
                nc.vector.memset(v_ones[u][:], 0.0).then_inc(v_clear.sem, 1)
            nc.vector.memset(k_stack["self"][:].rearrange("p a b t -> p (a b t)").bitcast(u32), 0)\
                .then_inc(stacks_clear.sem, 1)
            dve.wait_ge(v_clear.sem, 2)
            for u in US:
                last = nc.vector.memset(v_ones[u][:, :, :, DH0:DH0 + 1], 1.0)
            last.then_inc(stacks_set.sem, 1)
            dve.wait_ge(stacks_clear.sem, 2)
            for u in US:
                for hh in range(2):
                    rows = k_stack[u][STACK:ROWS, :, hh, :]
                    nc.vector.tensor_scalar(rows, rows, C[STACK:ROWS, C_ONES + hh:C_ONES + hh + 1], None, ALU.add)\
                        .then_inc(ones_set.sem, 1)

            def ln_apply(i, n):
                dve.wait_ge(rooted[n].sem, rooted[n].at(i, 1))
                nc.vector.tensor_tensor(unit[n][:, :], ln_banks(n)[0], rstd[n][:, :], ALU.mult).then_inc(scaled[n].sem, 1)
                dve.wait_ge(scaled[n].sem, scaled[n].at(i, 1))
                outs = (("k", k_in), ("v", v_in)) if n == "ctx" else ((n, normed[n]),)
                for name, out in outs:
                    nc.vector.tensor_scalar(out[:, :], unit[n][:, :], vec(f"g_{name}"), vec(f"b_{name}"),
                                            ALU.mult, ALU.add).then_inc(affine[n].sem, 1)

            def split(i, bank, parts, rest, first, less, done):
                dve.wait_ge(first.sem, first.at(i, 1))
                nc.vector.tensor_tensor(rest[:, :], bank, parts[0][:, :], ALU.subtract).then_inc(less.sem, 1)
                dve.wait_ge(less.sem, less.at(i, 1))
                nc.vector.tensor_copy(parts[1][:, :], rest[:, :]).then_inc(done.sem, 1)
                dve.wait_ge(done.sem, done.at(i, 1))
                nc.vector.tensor_tensor(parts[2][:, :], rest[:, :], parts[1][:, :], ALU.subtract).then_inc(done.sem, 1)

            def q_proj(i, u):
                split(i, q_bank(u), q_part[u], q_rest[u], q_first[u], q_less[u], q_split[u])

            def k_proj(i, u):
                split(i, k_bank(u), k_part[u], k_rest[u], k_first[u], k_less[u], k_split[u])

            def place(i, u, g):
                dve.wait_ge(neg_turned[u].sem, neg_turned[u].at(i, g + 1))
                nc.vector.tensor_copy(q_stack[u][STACK:ROWS, 2 * g:2 * g + 2, :],
                                      neg_rows[STACK:ROWS, 0:2 * TQ].rearrange("p (a q) -> p a q", a=2))\
                    .then_inc(neg_placed[u].sem, 1)

            def att(i, u, s, p):
                if p == TILES[u] // 2 + 1 and 0 <= s + 1 < GROUPS:
                    place(i, u, s + 1)
                g = s + 2
                if not 0 <= g < GROUPS:
                    return
                n = g * TILES[u] + p
                if p == 0 and g >= 2:
                    dve.wait_ge(neg_split[u].sem, neg_split[u].at(i, g - 1))
                dve.wait_ge(scores[u].sem, scores[u].at(i, n + 1))
                if u == "self":
                    out, src = neg_max[:, g % 2, :, p], ps[:, n % 2, :].rearrange("p (a k) -> p a k", a=QT)
                else:
                    out, src = neg_max[:, g % 2, p % QT, p // QT:p // QT + 1], ps[:, n % 2, :]
                nc.vector.tensor_reduce(out, src, AX, ALU.max, negate=True).then_inc(maxed[u].sem, 1)

            def att_norm(i, u):
                for qt in range(QT):
                    turned = ps[:, 2 + qt, :].rearrange("p (h c) -> p h c", c=V_WIDTH)
                    dve.wait_ge(heads_turned[u].sem, heads_turned[u].at(i, qt + 1))
                    nc.vector.reciprocal(recip[:, qt, :], turned[:, :, DH0]).then_inc(inverted[u].sem, 1)
                    dve.wait_ge(inverted[u].sem, inverted[u].at(i, qt + 1))
                    nc.vector.tensor_tensor(heads[:, qt, :, :], turned[:, :, 0:DH0],
                                            recip[:, qt, :].unsqueeze(2).to_broadcast([P, H0, DH0]), ALU.mult)\
                        .then_inc(divided[u].sem, 1)

            def att_wo(i, u):
                before = normed["in" if u == "self" else "mid"]
                dve.wait_ge(projected[u].sem, projected[u].at(i, 1))
                nc.vector.tensor_tensor(attended[u][:, :], ps[:, 4, 0:TQ], before[:, :], ALU.add)\
                    .then_inc(residual[u].sem, 1)

            def ffn_down(i):
                reuse(dve, b_residual["self"], i)
                dve.wait_ge(ffn_summed.sem, ffn_summed.at(i, 1))
                nc.vector.scalar_tensor_tensor(x_mid[:, :], ps[:, 2, 0:TQ], vec("b2"), attended["cross"][:, :],
                                               ALU.add, ALU.add).then_inc(layer0_done.sem, 1)

            def b_v(i, u):
                dve.wait_ge(b_v_made[u].sem, b_v_made[u].at(i, 1))
                nc.vector.tensor_copy(bv[:, 0:T_KEYS[u] // P, :], b_v_bank(u)).then_inc(b_v_kept[u].sem, 1)

            def b_score(i, u, t):
                dve.wait_ge(b_scores[u].sem, b_scores[u].at(i, t + 1))
                if u == "self":
                    out, src = b_neg[:, t, :], ps[:, 6 + t % 2, :].rearrange("p (a k) -> p a k", a=QT)
                else:
                    out, src = b_neg[:, t // QT, t % QT:t % QT + 1], ps[:, 6 + t % 2, :]
                nc.vector.tensor_reduce(out, src, AX, ALU.max, negate=True).then_inc(b_maxed[u].sem, 1)

            def b_norm(i, u, t):
                for h, qt in b_tile(u, t):
                    if qt == 0:
                        dve.wait_ge(b_exped[u].sem, b_exped[u].at(i, QT * (h + 1)))
                        nc.vector.reciprocal(b_rec[:, h, :], b_sum[:, h, :]).then_inc(b_inverted[u].sem, 1)
                        dve.wait_ge(b_inverted[u].sem, b_inverted[u].at(i, h + 1))
                    rows = b_probs[:, h, qt, 0:T_KEYS[u]]
                    nc.vector.tensor_scalar(rows, rows, b_rec[:, h, qt:qt + 1], None, ALU.mult)\
                        .then_inc(b_normed[u].sem, 1)

            def b_wo(i, u):
                before = x_mid if u == "self" else b_out["self"]
                dve.wait_ge(b_projected[u].sem, b_projected[u].at(i, 1))
                nc.vector.tensor_tensor(b_attended[u][:, :], ps[:, 7, 0:TQ], before[:, :], ALU.add)\
                    .then_inc(b_residual[u].sem, 1)

            def b_mlp(i, u, m):
                dve.wait_ge(b_gate_exp[u].sem, b_gate_exp[u].at(i, m + 1))
                nc.vector.tensor_scalar(b_gate[:, m, :], b_exp[:, m, :], 1.0, None, ALU.add).then_inc(b_gate_one[u].sem, 1)
                dve.wait_ge(b_gate_one[u].sem, b_gate_one[u].at(i, m + 1))
                nc.vector.reciprocal(b_exp[:, m, :], b_gate[:, m, :]).then_inc(b_gate_inv[u].sem, 1)
                dve.wait_ge(b_gate_inv[u].sem, b_gate_inv[u].at(i, m + 1))
                nc.vector.tensor_tensor(b_gate[:, m, :], ps[:, 6, :], b_exp[:, m, :], ALU.mult)\
                    .then_inc(b_gate_silu[u].sem, 1)
                dve.wait_ge(b_gate_silu[u].sem, b_gate_silu[u].at(i, m + 1))
                dve.wait_ge(b_up_made[u].sem, b_up_made[u].at(i, m + 1))
                nc.vector.tensor_tensor(b_hidden[:, 2 * m:2 * m + 2, :],
                                        ps[:, 7, :].rearrange("p (t q) -> p t q", t=2),
                                        b_gate[:, m, :].rearrange("p (t q) -> p t q", t=2), ALU.mult)\
                    .then_inc(b_hidden_kept[u].sem, 1)

            def b_down(i, u):
                dve.wait_ge(b_down_made[u].sem, b_down_made[u].at(i, 1))
                if u == "cross":
                    reuse(dve, stored, i)
                nc.vector.tensor_tensor(b_out[u][:, :], ps[:, 6, 0:TQ], b_attended[u][:, :], ALU.add)\
                    .then_inc(b_done[u].sem, 1)

            run(dve, dict(ln_apply=ln_apply, q_proj=q_proj, k_proj=k_proj, att=att, att_norm=att_norm,
                          att_wo=att_wo, ffn_down=ffn_down, b_v=b_v, b_score=b_score, b_norm=b_norm,
                          b_wo=b_wo, b_mlp=b_mlp, b_down=b_down))

        @block.tensor
        def _(pe):
            mm = nc.tensor.matmul

            def ln_centre(i, n):
                src, ready, k = LN_SRC[n]
                if n == "in":
                    reuse(pe, layer0_done, i)
                    if isinstance(i, int):
                        pe.wait_ge(const_loaded.sem, 16)
                pe.wait_ge(ready.sem, ready.at(i, k))
                mm(ln_banks(n)[0], centre, src[:, :], start=True, stop=True).then_inc(centred[n].sem, 1)

            def ln_var(i, n):
                pe.wait_ge(squared[n].sem, squared[n].at(i, 1))
                mm(ln_banks(n)[1], mean, square[n][:, :], start=True, stop=True).then_inc(variance[n].sem, 1)

            def q_proj(i, u):
                src, ready = Q_SRC[u]
                if u == "self" and isinstance(i, int):
                    pe.wait_ge(w_first_loaded.sem, 16)
                pe.wait_ge(ready.sem, ready.at(i, 1))
                mm(q_bank(u), w(f"{u}_wq"), src[:, :], start=True, stop=True).then_inc(q_made[u].sem, 1)

            def k_proj(i, u):
                src, ready = K_SRC[u]
                pe.wait_ge(ready.sem, ready.at(i, 1))
                mm(k_bank(u), w(f"{u}_wk"), src[:, :], start=True, stop=True).then_inc(k_made[u].sem, 1)

            def v_proj(i, u):
                src, ready = V_SRC[u]
                pe.wait_ge(ready.sem, ready.at(i, 1 if u == "self" else 2))
                for t in range(T_KEYS[u] // P):
                    last = mm(v_bank(u)[:, t * P:(t + 1) * P], src[:, t * P:(t + 1) * P], w(f"{u}_wv"),
                              start=True, stop=True)
                last.then_inc(v_made[u].sem, 1)

            def exp_scores(i, u, g, p):
                n = g * TILES[u] + p
                if p == 0:
                    pe.wait_ge(neg_placed[u].sem, neg_placed[u].at(i, g + 1))
                if n >= 2:
                    pe.wait_ge(exped[u].sem, exped[u].at(i, n - 1))
                per_head = T_KEYS[u] // 256
                h = GROUP * g + p // per_head
                for t in range(2):
                    k = P * (2 * (p % per_head) + t)
                    last = mm(ps[:, 2 + n % 2, t * TQ:(t + 1) * TQ], k_stack[u][0:ROWS, h // 2, h % 2, k:k + P],
                              q_stack[u][0:ROWS, h // 2, :], start=True, stop=True)
                last.then_inc(scores_t[u].sem, 1)

            def max_scores(i, u, g, p):
                n = g * TILES[u] + p
                if n == 0:
                    pe.wait_ge(q_stacked[u].sem, q_stacked[u].at(i, 16 * PRODUCTS))
                    pe.wait_ge(k_stacked[u].sem, k_stacked[u].at(i, 32 * PRODUCTS))
                    if u == "self":
                        if isinstance(i, int):
                            pe.wait_ge(ones_set.sem, 4)
                        pe.wait_ge(k_less["cross"].sem, k_less["cross"].at(i, 1))
                        pe.wait_ge(v_kept["cross"].sem, v_kept["cross"].at(i, 1))
                if n >= 2:
                    pe.wait_ge(maxed[u].sem, maxed[u].at(i, n - 1))
                if u == "self":
                    h = GROUP * g + p
                    for qt in range(QT):
                        last = mm(ps[:, n % 2, qt * TQ:(qt + 1) * TQ], q_stack[u][0:STACK, h // 2, qt * P:(qt + 1) * P],
                                  k_stack[u][0:STACK, h // 2, h % 2, :], start=True, stop=True)
                else:
                    h, qt = GROUP * g + p // QT, p % QT
                    last = mm(ps[:, n % 2, :], q_stack[u][0:STACK, h // 2, qt * P:(qt + 1) * P],
                              k_stack[u][0:STACK, h // 2, h % 2, :], start=True, stop=True)
                last.then_inc(scores[u].sem, 1)

            def weigh(i, u, g, p):
                kts = T_KEYS[u] // P
                if p == 0:
                    pe.wait_ge(exped[u].sem, exped[u].at(i, TILES[u] * (g + 1)))
                    if g == 0:
                        pe.wait_ge(v_kept[u].sem, v_kept[u].at(i, 1))
                    else:
                        pe.wait_ge(heads_kept[u].sem, heads_kept[u].at(i, g))
                for m in (2 * p, 2 * p + 1):
                    kt, j = m // GROUP, m % GROUP
                    last = mm(ps[32 * j:32 * j + V_WIDTH, 4, 0:TQ], v_ones[u][:, kt, GROUP * g + j, :],
                              probs_t[:, g % 2, j, kt, :], start=kt == 0, stop=kt == kts - 1,
                              tile_position=(0, 32 * j))
                if p == TILES[u] - 1:
                    last.then_inc(weighted[u].sem, 1)

            def turn_max(i, u, g):
                pe.wait_ge(neg_split[u].sem, neg_split[u].at(i, g + 1))
                if g:
                    pe.wait_ge(neg_placed[u].sem, neg_placed[u].at(i, g))
                elif isinstance(i, int) and u == "self":
                    pe.wait_ge(stacks_set.sem, 2)
                for pair in range(2):
                    for qt in range(QT):
                        at = pair * TQ + qt * P
                        last = nc.tensor.transpose(
                            neg_rows[STACK:ROWS, at:at + P],
                            neg_part[:, g % 2, qt, 2 * pair:2 * pair + 2, :].rearrange("p a b -> p (a b)"),
                            ident16[:, :])
                last.then_inc(neg_turned[u].sem, 1)

            def att(i, u, s, p):
                if 0 <= s < GROUPS:
                    exp_scores(i, u, s, p)
                if 0 <= s + 2 < GROUPS:
                    max_scores(i, u, s + 2, p)
                if 0 <= s - 1 < GROUPS:
                    weigh(i, u, s - 1, p)
                if p == TILES[u] // 2 and 0 <= s + 1 < GROUPS:
                    turn_max(i, u, s + 1)

            def att_turn(i, u):
                pe.wait_ge(heads_kept[u].sem, heads_kept[u].at(i, GROUPS))
                for qt in range(QT):
                    for g in range(GROUPS):
                        last = nc.tensor.transpose(ps[:, 2 + qt, g * P:(g + 1) * P],
                                                   heads_t[:, g, qt * P:(qt + 1) * P], ident)
                    last.then_inc(heads_turned[u].sem, 1)

            def att_back(i, u):
                for qt in range(QT):
                    pe.wait_ge(divided[u].sem, divided[u].at(i, qt + 1))
                    last = nc.tensor.transpose(ps[:, 5, qt * P:(qt + 1) * P],
                                               heads[:, qt, :, :].rearrange("p h d -> p (h d)"), ident)
                last.then_inc(heads_back[u].sem, 1)

            def att_wo(i, u):
                if isinstance(i, int) and u == "self":
                    pe.wait_ge(w_rest_loaded.sem, 16)
                pe.wait_ge(heads_done[u].sem, heads_done[u].at(i, 1))
                mm(ps[:, 4, 0:TQ], w(f"{u}_wo"), heads_f[:, :], start=True, stop=True).then_inc(projected[u].sem, 1)

            def ffn_up(i, m):
                pe.wait_ge(affine["out"].sem, affine["out"].at(i, 1))
                for t in range(2):
                    last = mm(ps[:, m, t * TQ:(t + 1) * TQ], w("w1", 2 * m + t), normed["out"][:, :],
                              start=True, stop=True)
                last.then_inc(ffn_made.sem, 1)

            def ffn_down(i):
                for t in range(DF // P):
                    pe.wait_ge(ffn_kept.sem, ffn_kept.at(i, t + 1))
                    last = mm(ps[:, 2, 0:TQ], w("w2", t), hidden[:, t, :], start=t == 0, stop=t == DF // P - 1)
                last.then_inc(ffn_summed.sem, 1)

            def b_source(u):
                return (x_mid, layer0_done) if u == "self" else (b_out["self"], b_done["self"])

            def b_k(i, u):
                if u == "self":
                    if isinstance(i, int):
                        pe.wait_ge(layer0_done.sem, layer0_done.at(i, 1))
                    else:
                        pe.wait_ge(layer0_done.sem, layer0_done.at(i, 1))
                        pe.wait_ge(w_layer1_loaded.sem, 16)
                    reuse(pe, b_done["cross"], i)
                    src = x_mid
                else:
                    pe.wait_ge(ctx1_loaded.sem, ctx1_loaded.at(i, 16))
                    pe.wait_ge(b_done["self"].sem, b_done["self"].at(i, 1))
                    src = ctx1
                mm(b_k_bank(u), w(f"b_{u}_wk"), src[:, :], start=True, stop=True).then_inc(b_k_made[u].sem, 1)

            def b_v(i, u):
                src = x_mid if u == "self" else ctx1
                for t in range(T_KEYS[u] // P):
                    last = mm(b_v_bank(u)[:, t, :], src[:, t * P:(t + 1) * P], w(f"b_{u}_wv"), start=True, stop=True)
                last.then_inc(b_v_made[u].sem, 1)

            def b_q(i, u):
                src, ready = b_source(u)
                pe.wait_ge(ready.sem, ready.at(i, 1))
                pe.wait_ge(b_k_kept[u].sem, b_k_kept[u].at(i, 1))
                mm(b_q_bank(u), w(f"b_{u}_wq"), src[:, :], start=True, stop=True).then_inc(b_q_made[u].sem, 1)

            def b_score(i, u, t):
                if t == 0:
                    pe.wait_ge(b_q_kept[u].sem, b_q_kept[u].at(i, 1))
                elif t == 1:
                    pe.wait_ge(b_v_kept[u].sem, b_v_kept[u].at(i, 1))
                else:
                    pe.wait_ge(b_exped[u].sem, b_exped[u].at(i, t - 1))
                for h, qt in b_tile(u, t):
                    f = slice(DH1 * h, DH1 * h + DH1)
                    last = mm(b_score_bank(u, t, qt), bq[f, qt * P:(qt + 1) * P], bk[f, 0:T_KEYS[u]],
                              start=True, stop=True, tile_position=(DH1 * h, 0))
                last.then_inc(b_scores[u].sem, 1)

            def b_turn(i, u, m):
                per_head = T_KEYS[u] // 256
                h = m // per_head
                if m < 2:
                    pe.wait_ge(b_exped[u].sem, b_exped[u].at(i, H1 * QT if m else H1 * QT - 1))
                else:
                    pe.wait_ge(b_turned_kept[u].sem, b_turned_kept[u].at(i, m - 1))
                pe.wait_ge(b_normed[u].sem, b_normed[u].at(i, QT * (h + 1)))
                for t in range(2):
                    kt = 2 * (m % per_head) + t
                    for qt in range(QT):
                        at = t * TQ + qt * P
                        last = nc.tensor.transpose(ps[:, 6 + m % 2, at:at + P],
                                                   b_probs[:, h, qt, kt * P:(kt + 1) * P], ident)
                last.then_inc(b_turned[u].sem, 1)

            def b_pv(i, u):
                pe.wait_ge(b_turned_kept[u].sem, b_turned_kept[u].at(i, N1[u]))
                kts = T_KEYS[u] // P
                for kt in range(kts):
                    for h in range(H1):
                        f = slice(DH1 * h, DH1 * h + DH1)
                        last = mm(ps[f, 6, 0:TQ], bv[:, kt, f], b_probs_t[:, h, kt, :],
                                  start=kt == 0, stop=kt == kts - 1, tile_position=(0, DH1 * h))
                last.then_inc(b_weighted[u].sem, 1)

            def b_wo(i, u):
                pe.wait_ge(b_heads_kept[u].sem, b_heads_kept[u].at(i, 1))
                mm(ps[:, 7, 0:TQ], w(f"b_{u}_wo"), b_heads[:, :], start=True, stop=True).then_inc(b_projected[u].sem, 1)

            def b_mlp(i, u, m):
                if m == 0:
                    pe.wait_ge(b_residual[u].sem, b_residual[u].at(i, 1))
                else:
                    pe.wait_ge(b_gate_silu[u].sem, b_gate_silu[u].at(i, m))
                for t in range(2):
                    last = mm(ps[:, 6, t * TQ:(t + 1) * TQ], w(f"b_{u}_wg", 2 * m + t), b_attended[u][:, :],
                              start=True, stop=True)
                last.then_inc(b_gate_made[u].sem, 1)
                if m:
                    pe.wait_ge(b_hidden_kept[u].sem, b_hidden_kept[u].at(i, m))
                for t in range(2):
                    last = mm(ps[:, 7, t * TQ:(t + 1) * TQ], w(f"b_{u}_wu", 2 * m + t), b_attended[u][:, :],
                              start=True, stop=True)
                last.then_inc(b_up_made[u].sem, 1)

            def b_down(i, u):
                for t in range(DF // P):
                    if t % 2 == 0:
                        pe.wait_ge(b_hidden_kept[u].sem, b_hidden_kept[u].at(i, t // 2 + 1))
                    if t == 0:
                        pe.wait_ge(b_gate_silu[u].sem, b_gate_silu[u].at(i, 2))
                    last = mm(ps[:, 6, 0:TQ], w(f"b_{u}_wd", t), b_hidden[:, t, :], start=t == 0, stop=t == DF // P - 1)
                last.then_inc(b_down_made[u].sem, 1)

            run(pe, dict(ln_centre=ln_centre, ln_var=ln_var, q_proj=q_proj, k_proj=k_proj, v_proj=v_proj, att=att,
                         att_turn=att_turn, att_back=att_back, att_wo=att_wo, ffn_up=ffn_up, ffn_down=ffn_down,
                         b_k=b_k, b_v=b_v, b_q=b_q, b_score=b_score, b_turn=b_turn, b_pv=b_pv, b_wo=b_wo,
                         b_mlp=b_mlp, b_down=b_down))




def kernel(**inputs):
    import numpy as np
    import concourse.bacc as bacc
    from concourse.bass_utils import run_bass_kernel_spmd

    fp32 = mybir.dt.float32
    a = {k: np.asarray(v) for k, v in inputs.items()}
    x_t = np.ascontiguousarray(a["x"].reshape(B * TQ, D).T)
    ctx_t = np.ascontiguousarray(a["ctx_1024"].reshape(B * TC, D).T)

    by_pair = np.arange(D).reshape(PAIRS, 2, DH0).transpose(1, 2, 0).reshape(-1)

    def tiles(m):
        return m.reshape(-1, P, m.shape[1]).transpose(1, 0, 2).reshape(P, -1)

    w = {}
    for u, s in (("self", "sa"), ("cross", "ca")):
        for n in "qkvo":
            t = a[f"L0_xattn_{s}_w{n}"].T
            w[f"{u}_w{n}"] = t[:, by_pair] if n in "qk" else t
            w[f"b_{u}_w{n}"] = a[f"L1_xattn_{s}_w{n}"]
        for n in "gu":
            w[f"b_{u}_w{n}"] = a[f"L1_xattn_{s}mlp_w{n}"]
        w[f"b_{u}_wd"] = tiles(a[f"L1_xattn_{s}mlp_wd"])
    w["w1"] = a["L0_xattn_ffn_w1"].T
    w["w2"] = tiles(a["L0_xattn_ffn_w2"].T)
    w_all = np.ascontiguousarray(np.concatenate([w[n] for n, _ in WEIGHTS], axis=1))

    source = {"g_in": "g_sa", "b_in": "b_sa", "g_k": "g_kca", "b_k": "b_kca", "g_v": "g_vca", "b_v": "b_vca",
              "g_mid": "g_qca", "b_mid": "b_qca", "g_out": "g_out", "b_out": "b_out", "b2": "ffn_b2", "b1": "ffn_b1"}
    vectors = np.concatenate([a[f"L0_xattn_{source[n]}"].reshape(-1, P) for n in VECTORS]).T
    ones = np.zeros((P, 2), np.float32)
    ones[STACK:STACK + 3, 0] = 1
    ones[STACK + 3:ROWS, 1] = 1
    c_all = np.ascontiguousarray(np.concatenate(
        [np.eye(P, dtype=np.float32) - np.float32(1 / D), np.full((P, P), 1 / D, np.float32),
         np.eye(P, dtype=np.float32), ones, vectors], axis=1))

    nc = bacc.Bacc("TRN2", target_bir_lowering=False, num_devices=1)
    arrays = {"x_t": x_t, "ctx_t": ctx_t, "w_all": w_all, "c_all": c_all}
    args = [nc.dram_tensor(n, v.shape, fp32, kind="ExternalInput").ap() for n, v in arrays.items()]
    out = nc.dram_tensor("out_t", (D, B * TQ), fp32, kind="ExternalOutput").ap()
    two_layers(nc, *args, out)
    r = run_bass_kernel_spmd(nc, [arrays], core_ids=[0])
    return np.ascontiguousarray(r.results[0]["out_t"].T).reshape(B, TQ, D)
```
